# Optimizing a Trainium2 kernel written in Bass

```python
import numpy as np
import jax
import jax.numpy as jnp

def _softmax(x, axis=-1):
    return jax.nn.softmax(x, axis=axis)

def _gelu(x):
    return jax.nn.gelu(x, approximate=True)

def _silu(x):
    return jax.nn.silu(x)

def _sigmoid(x):
    return jax.nn.sigmoid(x)

def _layernorm(x, axis=-1, eps=1e-05):
    m = jnp.mean(x, axis=axis, keepdims=True)
    v = jnp.var(x, axis=axis, keepdims=True)
    return (x - m) / jnp.sqrt(v + eps)

def _scatter_add(tgt, idx, src, axis=0):
    return tgt.at[idx].add(src)

def _segment_sum(src, seg, n):
    return jax.ops.segment_sum(src, seg, n)
kernel_name = 'mk_adj_resnorm_d2_adj_r2_9432c3'

def setup_inputs(seed: int=0):
    np.random.seed(seed)
    _w = jnp.asarray

    def _rec_inputs():
        import jax
        import jax.numpy as jnp
        _gk = jax.random.key(seed)
        x = 0.0001732 + 1 * jax.random.normal(jax.random.fold_in(_gk, 1), (5120, 64), jnp.float32)
        _a = jax.random.bernoulli(jax.random.fold_in(_gk, 2), 0.003125, (5120, 5120))
        _a = jnp.logical_or(_a, jnp.swapaxes(_a, -1, -2))
        _a = jnp.logical_or(_a, jnp.eye(5120, dtype=bool))
        _af = _a.astype(jnp.float32)
        _af = _af * jax.random.uniform(jax.random.fold_in(_gk, 3), (5120, 5120), jnp.float32, 0.05, 0.02)
        adj = _af
        return (x, adj)
    x, adj = _rec_inputs()

    def _L0_gnn_setup():
        import jax, jax.numpy as jnp
        import numpy as np
        N_USERS = 2048
        N_ITEMS = 3072
        EMB = 64
        LN_EPS = 1e-05
        key = jax.random.key(seed)
        ks = jax.random.split(key, 10)
        N = N_USERS + N_ITEMS
        ego = jax.random.normal(ks[0], (N, EMB), jnp.float32)
        adj = (jax.random.uniform(ks[1], (N, N), jnp.float32) < 0.01).astype(jnp.float32) * 0.02
        xav = float(np.sqrt(6.0 / (EMB + EMB)))
        W_u = jax.random.uniform(ks[2], (EMB, EMB), jnp.float32, -xav, xav)
        W_i = jax.random.uniform(ks[3], (EMB, EMB), jnp.float32, -xav, xav)
        diag_u = jax.random.uniform(ks[4], (N_USERS,), jnp.float32, 0.99, 1.01)
        diag_i = jax.random.uniform(ks[5], (N_ITEMS,), jnp.float32, 0.99, 1.01)
        par_u = jax.random.uniform(ks[6], (2,), jnp.float32, 0.0, 0.99)
        par_i = jax.random.uniform(ks[7], (2,), jnp.float32, 0.0, 0.99)
        ln_gamma = jnp.ones((EMB,), jnp.float32)
        ln_beta = jnp.zeros((EMB,), jnp.float32)
        return {'ego_embeddings': ego, 'adj': adj, 'W_u': W_u, 'diag_u': diag_u, 'par_u': par_u, 'W_i': W_i, 'diag_i': diag_i, 'par_i': par_i, 'ln_gamma': ln_gamma, 'ln_beta': ln_beta}
    _L0_gnn_all = _L0_gnn_setup()
    _L0_gnn_in = {k: v for k, v in _L0_gnn_all.items() if k in ('W_u', 'diag_u', 'par_u', 'W_i', 'diag_i', 'par_i', 'ln_gamma', 'ln_beta')}
    del _L0_gnn_all

    def _L1_gnn_setup():
        import jax, jax.numpy as jnp
        import numpy as np
        N = 8192
        F_IN = 64
        F_OUT = 64
        key = jax.random.key(seed)
        k1, k2, k3 = jax.random.split(key, 3)
        x = jax.random.normal(k1, (N, F_IN), dtype=jnp.float32)
        adj = jax.random.randint(k2, (N, N), 0, 2).astype(jnp.float32)
        W = jax.random.normal(k3, (F_IN, F_OUT), dtype=jnp.float32) * (1.0 / np.sqrt(F_IN))
        b = jnp.zeros((F_OUT,), dtype=jnp.float32)
        return {'x': x, 'adj': adj, 'W': W, 'b': b}
    _L1_gnn_all = _L1_gnn_setup()
    _L1_gnn_in = {k: v for k, v in _L1_gnn_all.items() if k in ('W', 'b')}
    del _L1_gnn_all
    return {'x': x, 'adj': adj, 'L0_gnn_W_u': _L0_gnn_in['W_u'], 'L0_gnn_diag_u': _L0_gnn_in['diag_u'], 'L0_gnn_par_u': _L0_gnn_in['par_u'], 'L0_gnn_W_i': _L0_gnn_in['W_i'], 'L0_gnn_diag_i': _L0_gnn_in['diag_i'], 'L0_gnn_par_i': _L0_gnn_in['par_i'], 'L0_gnn_ln_gamma': _L0_gnn_in['ln_gamma'], 'L0_gnn_ln_beta': _L0_gnn_in['ln_beta'], 'L1_gnn_W': _L1_gnn_in['W'], 'L1_gnn_b': _L1_gnn_in['b']}

def reference(x, adj, L0_gnn_W_u, L0_gnn_diag_u, L0_gnn_par_u, L0_gnn_W_i, L0_gnn_diag_i, L0_gnn_par_i, L0_gnn_ln_gamma, L0_gnn_ln_beta, L1_gnn_W, L1_gnn_b):
    import jax
    import jax.numpy as jnp

    def _L0_gnn_ref(ego_embeddings, adj, W_u, diag_u, par_u, W_i, diag_i, par_i, ln_gamma, ln_beta):
        import jax, jax.numpy as jnp
        import numpy as np
        N_USERS = 2048
        N_ITEMS = 3072
        EMB = 64
        LN_EPS = 1e-05
        nu = diag_u.shape[0]
        res = ego_embeddings
        ego_u = ego_embeddings[:nu]
        ego_i = ego_embeddings[nu:]
        u = par_u[0] * par_u[1] * (diag_u[:, None] * ego_u @ W_u) + ego_u
        i = par_i[0] * par_i[1] * (diag_i[:, None] * ego_i @ W_i) + ego_i
        e = jnp.concatenate([u, i], axis=0)
        h = adj @ (adj.T @ e)
        mu = jnp.mean(h, axis=-1, keepdims=True)
        var = jnp.var(h, axis=-1, keepdims=True)
        out = (h - mu) * jax.lax.rsqrt(var + LN_EPS) * ln_gamma + ln_beta + res
        return out

    def _L1_gnn_ref(x, adj, W, b):
        import jax, jax.numpy as jnp
        import numpy as np
        N = 8192
        F_IN = 64
        F_OUT = 64
        deg = adj.sum(axis=0) + 1.0
        dinv = jnp.where(deg > 0, jax.lax.rsqrt(deg), 0.0)
        xw = x @ W
        z = dinv[:, None] * xw
        out = dinv[:, None] * (adj.T @ z + z) + b
        return jax.nn.relu(out)
    x = _layernorm(x + _L0_gnn_ref(x, adj, L0_gnn_W_u, L0_gnn_diag_u, L0_gnn_par_u, L0_gnn_W_i, L0_gnn_diag_i, L0_gnn_par_i, L0_gnn_ln_gamma, L0_gnn_ln_beta), axis=-1)
    x = _layernorm(x + _L1_gnn_ref(x, adj, L1_gnn_W, L1_gnn_b), axis=-1)
    return x

_drawn_inputs = setup_inputs


def setup_inputs(seed=0):
    import zlib

    import numpy as np

    out = dict(_drawn_inputs(seed))
    spreads = {'L0_gnn_ln_gamma': (1.0, 0.2), 'L0_gnn_ln_beta': (0.0, 0.1), 'L1_gnn_b': (0.0, 0.1)}
    factors = {'L0_gnn_diag_u': 8.0, 'L0_gnn_W_i': 5.668, 'L0_gnn_diag_i': 8.0}
    for name, (base, spread) in spreads.items():
        noise = np.random.default_rng([zlib.crc32(name.encode()), seed]).standard_normal(out[name].shape)
        drawn = base * np.exp(spread * noise) if base else spread * noise
        out[name] = jnp.asarray(drawn.astype(out[name].dtype))
    for name, factor in factors.items():
        out[name] = (out[name] * factor).astype(out[name].dtype)
    return out
```

```python
import concourse.bass as bass
from concourse import mybir
from contextlib import ExitStack

N = 5120
F = 64
P = 128
NB = N // P
JW = 512
JB = JW // P
NJ = N // JW
CB = 5
NQ = NB // CB
GB = 8
NG = NB // GB
RES = 2
USERS = 2048 // P
TPG = 5
EPS = 1e-5
NORMS = [("h", 0)] + [v for g in range(1, NG) for v in (("h", g), ("y", g - 1))] + [("y", NG - 1)]
ROOT_AFTER = [13, 21, 25, 29, 33, 37]
WARM = 4
MAIN_STEPS = 8


def build(nc, x, adj, W_u, diag_u, par_u, W_i, diag_i, par_i, gamma, beta, W1, b1, out):
    f32 = mybir.dt.float32
    bf16 = mybir.dt.bfloat16
    ALU = mybir.AluOpType
    ACT = mybir.ActivationFunctionType
    AX = mybir.AxisListType.X

    x_rows = x.rearrange("(b p) f -> p b f", p=P)
    out_rows = out.rearrange("(b p) f -> p b f", p=P)
    adj_rows = adj.rearrange("(b p) j -> p b j", p=P)

    ctx = ExitStack()
    with ctx:
        def sb(name, shape, dt=f32):
            return ctx.enter_context(nc.sbuf_tensor(name, shape, dt))

        def sem(name):
            return ctx.enter_context(nc.semaphore(name))

        tile = [[sb(f"adj_{s}_{q}", [P, CB, JW]) for q in range(NQ)] for s in range(RES)]
        X = sb("X", [P, NB, F])
        E = sb("E", [P, NB, F + 1])
        T = [sb(f"T{i}", [P, JB, F + 1]) for i in range(2)]
        adjT = [sb(f"adjT{i}", [P, JW]) for i in range(2)]
        xT = sb("xT", [P, GB * F])
        Y = [sb(f"Y{i}", [P, GB, F]) for i in range(2)]
        C = sb("C", [P, GB, F])
        SQ = sb("SQ", [P, GB, F])
        ident = sb("ident", [P, P])
        zeros = sb("zeros", [P, 512], bf16)
        Wd = sb("Wd", [P, 3, 2 * F])
        gamma_b = sb("gamma_b", [P, F])
        beta_b = sb("beta_b", [P, F])
        bias_b = sb("bias_b", [P, F])
        par = sb("par", [P, 4])
        par2 = sb("par2", [P, 2])
        diag = sb("diag", [NB, P])
        scale = sb("scale", [P, NB])
        deg = sb("deg", [P, NB])
        dinv = sb("dinv", [P, NB])
        mask = sb("mask", [P, NB])
        rsum = sb("rsum", [P, GB])
        var = sb("var", [P, GB])
        std = sb("std", [P, GB])
        rstd = sb("rstd", [P, GB])
        h_rstd = [sb(f"h_rstd{i}", [P, GB]) for i in range(2)]

        bank = [ctx.enter_context(nc.psum_tensor(f"bank{i}", [P, 512], f32)) for i in range(8)]
        h_acc = [bank[g][:, :].rearrange("p (b f) -> p b f", f=F) for g in range(NG)]
        out_acc = [bank[i][:, 0:JB * F].rearrange("p (b f) -> p b f", f=F) for i in range(4)]
        t_acc = bank[5][:, 0:JB * (F + 1)].rearrange("p (b f) -> p b f", f=F + 1)
        tr = [bank[6], bank[7]]
        xT_ps = bank[6]
        xw_ps = bank[7][:, :].rearrange("p (b f) -> p b f", f=F)

        x_loaded = [sem(f"x_loaded{g}") for g in range(NG)]
        consts_loaded = sem("consts_loaded")
        weights_loaded = sem("weights_loaded")
        adj_loaded = [[sem(f"adj_loaded_{s}_{q}") for q in range(NQ)] for s in range(RES)]
        chunk_used = sem("chunk_used")
        chunk_swept = sem("chunk_swept")
        out_stored = [sem(f"out_stored{i}") for i in range(2)]
        pool_chain = sem("pool_chain")
        weights_zeroed = sem("weights_zeroed")
        ident_ready = sem("ident_ready")
        zeros_ready = sem("zeros_ready")
        ones_ready = sem("ones_ready")
        diagT_done = sem("diagT_done")
        xT_done = sem("xT_done")
        xT_ready = sem("xT_ready")
        xw_done = sem("xw_done")
        e_ready = sem("e_ready")
        z_ready = sem("z_ready")
        residual_ready = sem("residual_ready")
        t_done = sem("t_done")
        t_ready = sem("t_ready")
        tr_done = [sem(f"tr_done{i}") for i in range(2)]
        adjT_ready = [sem(f"adjT_ready{i}") for i in range(2)]
        h_done = sem("h_done")
        bank_free = [sem(f"bank_free{i}") for i in range(NG)]
        h_squared = sem("h_squared")
        h_rstd_ready = sem("h_rstd_ready")
        var_ready = sem("var_ready")
        root_ready = sem("root_ready")
        normed = sem("normed")
        x1_ready = sem("x1_ready")
        dinv_sum = sem("dinv_sum")
        dinv_root = sem("dinv_root")
        acc_done = sem("acc_done")
        o_centred = sem("o_centred")
        o_squared = sem("o_squared")
        o_var = sem("o_var")
        o_root = sem("o_root")
        out_ready = sem("out_ready")
        dve_chain = sem("dve_chain")
        finish_chain = sem("finish_chain")

        def feat(v, n=GB):
            return v[:, :].unsqueeze(1).to_broadcast([P, n, F])

        def rows(v, n=GB):
            return v.unsqueeze(2).to_broadcast([P, n, F])

        block = ctx.enter_context(nc.Block())

        @block.sync
        def _(sp):
            def load(s, q, J):
                sp.dma_start(tile[s][q][:, :, :], adj_rows[:, q * CB:(q + 1) * CB, bass.ds(J * JW, JW)])\
                  .then_inc(adj_loaded[s][q], 16)

            for p in range(RES):
                for q in range(NQ):
                    load(p, q, RES + p)
                    if p == 0 and q == 0:
                        sp.wait_ge(weights_loaded, 16 * 6)
                        sp.wait_ge(consts_loaded, 16 * 7)
            with sp.Fori(0, (NJ - 2 * RES) // RES) as it:
                for s in range(RES):
                    for q in range(NQ):
                        sp.wait_ge(chunk_used, (it * RES + s) * NQ + q + 1)
                        load(s, q, it * RES + (2 * RES + s))
            for s in range(RES):
                for q in range(NQ):
                    sp.wait_ge(chunk_used, (NJ - 2 * RES + s) * NQ + q + 1)
                    load(s, q, s)
            with sp.Fori(1, NJ // RES) as k:
                for q in range(NQ):
                    for s in range(RES):
                        if q < NQ - 1:
                            sp.wait_ge(chunk_swept, (k - 1) * ((NQ - 1) * RES) + (q * RES + s + 1))
                        else:
                            sp.wait_ge(acc_done, (k - 1) * RES + (s + 1))
                        load(s, q, k * RES + s)

        @block.gpsimd
        def _(pool):
            chain = [0]

            def link(ins):
                chain[0] += 1
                ins.then_inc(pool_chain, 1)
                pool.wait_ge(pool_chain, chain[0])

            nc.gpsimd.memset(Wd[:, :, :], 0.0).then_inc(weights_zeroed, 1)
            link(nc.gpsimd.memset(ident[:, :], 0.0))
            nc.gpsimd.affine_select(out=ident[:, :], in_=ident[:, :], compare_op=ALU.not_equal, fill=1.0,
                                    base=0, pattern=[[-1, P]], channel_multiplier=1).then_inc(ident_ready, 1)
            nc.gpsimd.memset(E[:, :, F:F + 1], 1.0).then_inc(ones_ready, 1)
            nc.gpsimd.memset(zeros[:, :], 0.0).then_inc(zeros_ready, 1)
            pool.wait_ge(consts_loaded, 16 * 7)
            for g in range(NG):
                pool.wait_ge(e_ready, g + 1)
                Xg = X[:, g * GB:(g + 1) * GB, :]
                link(nc.gpsimd.tensor_scalar(Xg, Xg, 2.0, None, ALU.mult))
                nc.gpsimd.tensor_tensor(Xg, Xg, feat(beta_b), ALU.add).then_inc(residual_ready, 1)

            def norm_h(g):
                Yg = Y[g % 2][:, :, :]
                pool.wait_ge(bank_free[g], 1)
                nc.gpsimd.tensor_tensor(SQ[:, :, :], Yg, Yg, ALU.mult).then_inc(h_squared, 1)
                pool.wait_ge(h_rstd_ready, g + 1)
                link(nc.gpsimd.tensor_tensor(Yg, Yg, rows(h_rstd[g % 2][:, :]), ALU.mult))
                link(nc.gpsimd.tensor_tensor(Yg, Yg, feat(gamma_b), ALU.mult))
                if g == 0:
                    pool.wait_ge(residual_ready, NG)
                nc.gpsimd.tensor_tensor(Yg, Yg, X[:, g * GB:(g + 1) * GB, :], ALU.add).then_inc(normed, 1)

            for g in range(NG):
                norm_h(g)

        @block.scalar
        def _(act):
            for g in range(NG):
                act.dma_start(X[:, g * GB:(g + 1) * GB, :], x_rows[:, g * GB:(g + 1) * GB, :])\
                   .then_inc(x_loaded[g], 16)
                if g == 0:
                    act.dma_start(diag[0:USERS, :], diag_u.rearrange("(b p) -> b p", p=P)).then_inc(consts_loaded, 16)
                    act.dma_start(diag[USERS:NB, :], diag_i.rearrange("(b p) -> b p", p=P)).then_inc(consts_loaded, 16)
                    act.dma_start(par[:, 0:2], par_u.unsqueeze(0).to_broadcast([P, 2])).then_inc(consts_loaded, 16)
                    act.dma_start(par[:, 2:4], par_i.unsqueeze(0).to_broadcast([P, 2])).then_inc(consts_loaded, 16)
                    act.wait_ge(weights_zeroed, 1)
                    for i, w in enumerate((W_u, W_i, W1)):
                        for r in range(2):
                            act.dma_start(Wd[r * F:(r + 1) * F, i, r * F:(r + 1) * F], w)\
                               .then_inc(weights_loaded, 16)
            for v, d in ((gamma_b, gamma), (beta_b, beta), (bias_b, b1)):
                act.dma_start(v[:, :], d.unsqueeze(0).to_broadcast([P, F])).then_inc(consts_loaded, 16)

            def copy_xT(n):
                act.wait_ge(xT_done, n + 1)
                nc.scalar.activation(xT[:, :], xT_ps[:, :], ACT.Copy).then_inc(xT_ready, 1)

            def copy_adjT(e, n):
                act.wait_ge(tr_done[e], n + 1)
                nc.scalar.activation(adjT[e][:, :], tr[e][:, :], ACT.Copy).then_inc(adjT_ready[e], 1)

            for g in range(NG):
                copy_xT(g)
            with act.Fori(0, MAIN_STEPS) as step:
                for i in range(NB // 2):
                    copy_adjT(0, step * (NB // 2) + i)
            for i in range(NB // 2):
                copy_adjT(0, MAIN_STEPS * (NB // 2) + i)
            act.wait_ge(dinv_sum, 1)
            nc.scalar.activation(dinv[:, :], dinv[:, :], ACT.Sqrt).then_inc(dinv_root, 1)

            def root(n):
                act.wait_ge(var_ready, n + 1)
                nc.scalar.activation(std[:, :], var[:, :], ACT.Sqrt).then_inc(root_ready, 1)

            for b in range(NB):
                copy_adjT(b % 2, (NJ - 1) * (NB // 2) + b // 2)
                if b in ROOT_AFTER:
                    root(ROOT_AFTER.index(b))
            for g, n in enumerate(range(len(ROOT_AFTER), len(NORMS))):
                root(n)
                if g < 3:
                    copy_xT(NG + g)
            copy_xT(NG + 3)
            copy_xT(NG + 4)

            def finish(J, par_):
                act.wait_ge(o_centred, J + 1)
                nc.scalar.activation(Y[0][:, JB:2 * JB, :], Y[0][:, 0:JB, :], ACT.Square).then_inc(o_squared, 1)
                act.wait_ge(o_var, J + 1)
                nc.scalar.activation(std[:, 0:JB], var[:, 0:JB], ACT.Sqrt).then_inc(o_root, 1)
                act.wait_ge(out_ready, J + 1)
                act.dma_start(out_rows[:, bass.ds(J * JB, JB), :], Y[1][:, par_ * JB:(par_ + 1) * JB, :])\
                   .then_inc(out_stored[par_], 16)

            for J in range(RES):
                finish(J, J)
            with act.Fori(1, NJ // RES) as k:
                for s in range(RES):
                    finish(k * RES + s, s)
            for i in range(2):
                act.wait_ge(out_stored[i], 16 * (NJ // 2))

        @block.vector
        def _(dve):
            chain = [0]

            def link(ins):
                chain[0] += 1
                ins.then_inc(dve_chain, 1)
                dve.wait_ge(dve_chain, chain[0])

            v = nc.vector
            dve.wait_ge(consts_loaded, 16 * 7)
            link(v.tensor_tensor(par2[:, 0:1], par[:, 0:1], par[:, 1:2], ALU.mult))
            link(v.tensor_tensor(par2[:, 1:2], par[:, 2:3], par[:, 3:4], ALU.mult))
            dve.wait_ge(diagT_done, 1)
            link(v.tensor_scalar(scale[:, 0:USERS], bank[5][:, 0:USERS], par2[:, 0:1], None, ALU.mult))
            link(v.tensor_scalar(scale[:, USERS:NB], bank[5][:, USERS:NB], par2[:, 1:2], None, ALU.mult))
            for g in range(NG):
                b0, b1_ = g * GB, (g + 1) * GB
                dve.wait_ge(xw_done, g + 1)
                link(v.tensor_tensor(C[:, :, :], xw_ps, rows(scale[:, b0:b1_]), ALU.mult))
                link(v.tensor_tensor(C[:, :, :], C[:, :, :], X[:, b0:b1_, :], ALU.add))
                link(v.tensor_reduce(rsum[:, :], C[:, :, :], AX, ALU.add))
                v.scalar_tensor_tensor(E[:, b0:b1_, 0:F], rows(rsum[:, :]), -1.0 / F, C[:, :, :],
                                       ALU.mult, ALU.add).then_inc(e_ready, 1)

            def copy_t(step, i):
                dve.wait_ge(t_done, step + 1)
                v.tensor_copy(T[i][:, :, :], t_acc).then_inc(t_ready, 1)
                v.tensor_copy(deg[:, bass.ds(step * JB, JB)], t_acc[:, :, F]).then_inc(t_ready, 1)

            def copy_adjT(n):
                dve.wait_ge(tr_done[1], n + 1)
                v.tensor_copy(adjT[1][:, :], tr[1][:, :]).then_inc(adjT_ready[1], 1)

            def odd_blocks(step, i):
                for b in range(NB // 2):
                    copy_adjT(step * (NB // 2) + b)
                    if b == NB * JB // TPG // 2 - 1:
                        copy_t(step + 1, 1 - i)

            copy_t(0, 0)
            with dve.Fori(0, MAIN_STEPS // 2) as it:
                for i in range(2):
                    odd_blocks(it * 2 + i, i)
            odd_blocks(MAIN_STEPS, 0)

            dve.wait_ge(t_ready, 2 * NJ)
            late = RES * JB
            link(v.tensor_scalar(mask[:, late:NB], deg[:, 0:NB - late], 1.0, None, ALU.add))
            link(v.tensor_scalar(mask[:, 0:late], deg[:, NB - late:NB], 1.0, None, ALU.add))
            v.tensor_scalar(dinv[:, :], mask[:, :], 1.2e-38, None, ALU.max).then_inc(dinv_sum, 1)
            dve.wait_ge(dinv_root, 1)
            link(v.tensor_scalar(mask[:, :], mask[:, :], 0.0, None, ALU.is_gt))
            link(v.reciprocal(dinv[:, :], dinv[:, :]))
            link(v.tensor_tensor(dinv[:, :], dinv[:, :], mask[:, :], ALU.mult))

            def inverse_std(n, dst):
                v.tensor_scalar(var[:, :], rsum[:, :], 1.0 / F, EPS, ALU.mult, ALU.add).then_inc(var_ready, 1)
                dve.wait_ge(root_ready, n + 1)
                return v.reciprocal(dst, std[:, :])

            def stats_h(g, n):
                dve.wait_ge(h_done, g + 1)
                v.tensor_copy(Y[g % 2][:, :, :], h_acc[g]).then_inc(bank_free[g], 1)
                if g == NG - 1:
                    make_z(0)
                dve.wait_ge(h_squared, g + 1)
                link(v.tensor_reduce(rsum[:, :], SQ[:, :, :], AX, ALU.add))
                inverse_std(n, h_rstd[g % 2][:, :]).then_inc(h_rstd_ready, 1)

            def norm_y(g, n):
                dve.wait_ge(normed, g + 1)
                Yg = Y[g % 2][:, :, :]
                link(v.tensor_reduce(rsum[:, :], Yg, AX, ALU.add))
                link(v.scalar_tensor_tensor(C[:, :, :], rows(rsum[:, :]), -1.0 / F, Yg, ALU.mult, ALU.add))
                link(v.tensor_tensor(Yg, C[:, :, :], C[:, :, :], ALU.mult))
                link(v.tensor_reduce(rsum[:, :], Yg, AX, ALU.add))
                link(inverse_std(n, rstd[:, :]))
                v.tensor_tensor(X[:, g * GB:(g + 1) * GB, :], C[:, :, :], rows(rstd[:, :]), ALU.mult)\
                 .then_inc(x1_ready, 1)

            def make_z(g):
                dve.wait_ge(xw_done, NG + g + 1)
                v.tensor_tensor(E[:, g * GB:(g + 1) * GB, 0:F], xw_ps, rows(dinv[:, g * GB:(g + 1) * GB]),
                                ALU.mult).then_inc(z_ready, 1)

            for n, (what, g) in enumerate(NORMS):
                if what == "h":
                    stats_h(g, n)
                else:
                    norm_y(g, n)
                if (what, g) == ("y", NG - 2):
                    make_z(1)
            for g in range(2, NG):
                make_z(g)

            def finish(J, acc, freed, i, earlier):
                o, sq, r = Y[0][:, 0:JB, :], Y[0][:, JB:2 * JB, :], rstd[:, 0:JB]
                stage = Y[1][:, i * JB:(i + 1) * JB, :]
                blocks = bass.ds(J * JB, JB)

                def after(n, ins):
                    ins.then_inc(finish_chain, 1)
                    dve.wait_ge(finish_chain, J * 6 + n)

                dve.wait_ge(acc_done, J + 1)
                if earlier is not None or J > 0:
                    dve.wait_ge(out_ready, J)
                v.tensor_tensor(o, out_acc[acc], E[:, blocks, 0:F], ALU.add).then_inc(bank_free[acc], 1)
                dve.wait_ge(bank_free[acc], freed)
                after(1, v.tensor_tensor(o, o, rows(dinv[:, blocks], JB), ALU.mult))
                after(2, v.tensor_tensor(o, o, feat(bias_b, JB), ALU.add))
                after(3, v.scalar_tensor_tensor(o, o, 0.0, X[:, blocks, :], ALU.max, ALU.add))
                after(4, v.tensor_reduce(rsum[:, 0:JB], o, AX, ALU.add))
                v.scalar_tensor_tensor(o, rows(rsum[:, 0:JB], JB), -1.0 / F, o, ALU.mult, ALU.add)\
                 .then_inc(o_centred, 1)
                dve.wait_ge(o_squared, J + 1)
                after(5, v.tensor_reduce(rsum[:, 0:JB], sq, AX, ALU.add))
                v.tensor_scalar(var[:, 0:JB], rsum[:, 0:JB], 1.0 / F, EPS, ALU.mult, ALU.add).then_inc(o_var, 1)
                dve.wait_ge(o_root, J + 1)
                after(6, v.reciprocal(r, std[:, 0:JB]))
                if earlier is not None:
                    dve.wait_ge(out_stored[i], earlier * 16)
                v.tensor_tensor(stage, o, rows(r, JB), ALU.mult).then_inc(out_ready, 1)

            for s in range(RES):
                finish(s, s, 2, s, None)
            with dve.Fori(0, (NJ // RES - 1) // 2) as it:
                for k in (1, 2):
                    for s in range(RES):
                        finish((it * 2 + k) * RES + s, 2 * (k % 2) + s, it + (k + 1), s, it * 2 + k)

        @block.tensor
        def _(pe):
            mm = nc.tensor.matmul

            pe.wait_ge(ident_ready, 1)
            pe.wait_ge(consts_loaded, 16 * 7)
            nc.tensor.transpose(bank[5][:, 0:NB], diag[:, :], ident[0:NB, 0:NB]).then_inc(diagT_done, 1)
            pe.wait_ge(weights_loaded, 16 * 6)

            def transpose_rows(g):
                for i in range(GB // 2):
                    b = g * GB + 2 * i
                    last = nc.tensor.transpose(xT_ps[:, i * P:(i + 1) * P],
                                               X[:, b:b + 2, :].rearrange("p b f -> p (b f)"), ident[:, :])
                last.then_inc(xT_done, 1)

            def project(n, w):
                pe.wait_ge(xT_ready, n + 1)
                for i in range(GB // 2):
                    last = mm(bank[7][:, i * P:(i + 1) * P], xT[:, i * P:(i + 1) * P], Wd[:, w, :],
                              start=True, stop=True)
                last.then_inc(xw_done, 1)

            def t_product(s, b, jb):
                return mm(t_acc[:, jb, :], tile[s][b // CB][:, b % CB, jb * P:(jb + 1) * P], E[:, b, :],
                          start=(b == 0 and jb == 0), stop=(b == NB - 1), skip_group_check=True)

            def project_x(g):
                pe.wait_ge(x_loaded[g], 16)
                if g >= 1:
                    pe.wait_ge(xT_ready, g)
                transpose_rows(g)
                if g >= 1:
                    pe.wait_ge(e_ready, g)
                project(g, 0 if g * GB < USERS else 1)

            project_x(0)
            project_x(1)
            pe.wait_ge(zeros_ready, 1)
            for _ in range(WARM):
                for g in range(NG):
                    mm(bank[g][:, :], zeros[:, 0:P], zeros[:, :], start=True, stop=True)
            for g in range(NG):
                if g + 1 < NG and g > 0:
                    project_x(g + 1)
                if g == 0:
                    pe.wait_ge(ones_ready, 1)
                pe.wait_ge(e_ready, g + 1)
                for b in range(g * GB, (g + 1) * GB):
                    if b % CB == 0:
                        pe.wait_ge(adj_loaded[0][b // CB], 16)
                    for jb in range(JB):
                        last = t_product(0, b, jb)
            last.then_inc(t_done, 1)

            def transpose_adj(s, b):
                for jb in range(JB):
                    last = nc.tensor.transpose(tr[b % 2][:, jb * P:(jb + 1) * P],
                                               tile[s][b // CB][:, b % CB, jb * P:(jb + 1) * P], ident[:, :])
                last.then_inc(tr_done[b % 2], 1)

            def h_step(step, s, loads=None):
                pe.wait_ge(t_ready, step * 2 + 2)
                n = 0
                for b in range(NB):
                    if loads is not None and b * TPG < NB * JB:
                        for m in range(b * TPG, (b + 1) * TPG):
                            bt, jt = m // JB, m % JB
                            if m % (CB * JB) == 0:
                                pe.wait_ge(adj_loaded[1 - s][bt // CB], loads * 16)
                            last = t_product(1 - s, bt, jt)
                        if m == NB * JB - 1:
                            last.then_inc(t_done, 1)
                    if b + 1 < NB:
                        transpose_adj(s, b + 1)
                    elif loads is not None:
                        transpose_adj(1 - s, 0)
                    pe.wait_ge(adjT_ready[b % 2], step * (NB // 2) + (b // 2 + 1))
                    for jb in range(JB):
                        last = mm(h_acc[b // GB][:, b % GB, :], adjT[b % 2][:, jb * P:(jb + 1) * P],
                                  T[s][:, jb, 0:F], start=False, stop=False, skip_group_check=True)
                    if loads is not None and b % CB == CB - 1:
                        last.then_inc(chunk_used, 1)
                    if loads is None and b % GB == GB - 1:
                        last.then_inc(h_done, 1)

            pe.wait_ge(xT_ready, NG)
            transpose_adj(0, 0)
            with pe.Fori(0, MAIN_STEPS // 2) as it:
                h_step(it * 2, 0, it + 1)
                h_step(it * 2 + 1, 1, it + 2)
            h_step(MAIN_STEPS, 0, NJ // RES)
            h_step(NJ - 1, 1)

            def out_product(acc, s, b, jb):
                return mm(out_acc[acc][:, jb, :], tile[s][b // CB][:, b % CB, jb * P:(jb + 1) * P],
                          E[:, b, 0:F], start=(b == 0 and jb == 0), stop=(b == NB - 1), skip_group_check=True)

            def transpose_x1(g):
                pe.wait_ge(x1_ready, g + 1)
                pe.wait_ge(xT_ready, NG + g)
                transpose_rows(g)

            def project_x1(g):
                if g >= 1:
                    pe.wait_ge(z_ready, g)
                project(NG + g, 2)

            def first_round(lo, hi):
                for b in range(lo, hi):
                    if b % GB == 0:
                        pe.wait_ge(z_ready, b // GB + 1)
                    for s in range(RES):
                        for jb in range(JB):
                            last = out_product(s, s, b, jb)
                        if b == NB - 1:
                            last.then_inc(acc_done, 1)
                        elif b % CB == CB - 1:
                            last.then_inc(chunk_swept, 1)

            transpose_x1(0)
            project_x1(0)
            transpose_x1(1)
            project_x1(1)
            for s in range(RES):
                pe.wait_ge(bank_free[s], 1)
            transpose_x1(2)
            first_round(0, GB)
            project_x1(2)
            transpose_x1(3)
            first_round(GB, 2 * GB)
            project_x1(3)
            first_round(2 * GB, 3 * GB + GB // 2)
            transpose_x1(4)
            first_round(3 * GB + GB // 2, 4 * GB)
            project_x1(4)
            first_round(4 * GB, NB)

            with pe.Fori(0, (NJ // RES - 1) // 2) as it:
                for k in (1, 2):
                    for s in range(RES):
                        pe.wait_ge(bank_free[2 * (k % 2) + s], it + k)
                    for q in range(NQ):
                        for s in range(RES):
                            pe.wait_ge(adj_loaded[s][q], (it * 2 + k + NJ // RES) * 16)
                            for b in range(q * CB, (q + 1) * CB):
                                for jb in range(JB):
                                    last = out_product(2 * (k % 2) + s, s, b, jb)
                            last.then_inc(acc_done if q == NQ - 1 else chunk_swept, 1)


_INS = ['x', 'adj', 'L0_gnn_W_u', 'L0_gnn_diag_u', 'L0_gnn_par_u', 'L0_gnn_W_i', 'L0_gnn_diag_i',
        'L0_gnn_par_i', 'L0_gnn_ln_gamma', 'L0_gnn_ln_beta', 'L1_gnn_W', 'L1_gnn_b']


def kernel(**inputs):
    import numpy as _np
    import concourse.bacc as _bacc
    from concourse import mybir as _mybir
    from concourse.bass_utils import run_bass_kernel_spmd as _run

    nc = _bacc.Bacc("TRN2", target_bir_lowering=False, num_devices=1)
    arrays, args = {}, []
    for name in _INS:
        a = _np.ascontiguousarray(inputs[name])
        arrays[f"in_{name}_dram"] = a
        args.append(nc.dram_tensor(f"in_{name}_dram", a.shape, _mybir.dt.from_np(a.dtype), kind="ExternalInput").ap())
    args.append(nc.dram_tensor("out_dram", (N, F), _mybir.dt.float32, kind="ExternalOutput").ap())
    build(nc, *args)
    r = _run(nc, [arrays], core_ids=[0])
    return r.results[0]["out_dram"]
```
